# Optimizing a Trainium2 kernel written in Bass

```python
import numpy as np
import jax
import jax.numpy as jnp

def _softmax(x, axis=-1):
    return jax.nn.softmax(x, axis=axis)

def _gelu(x):
    return jax.nn.gelu(x, approximate=True)

def _silu(x):
    return jax.nn.silu(x)

def _sigmoid(x):
    return jax.nn.sigmoid(x)

def _layernorm(x, axis=-1, eps=1e-05):
    m = jnp.mean(x, axis=axis, keepdims=True)
    v = jnp.var(x, axis=axis, keepdims=True)
    return (x - m) / jnp.sqrt(v + eps)

def _scatter_add(tgt, idx, src, axis=0):
    return tgt.at[idx].add(src)

def _segment_sum(src, seg, n):
    return jax.ops.segment_sum(src, seg, n)
kernel_name = 'mk_dlrm_tower_d1_rec_r8_42e79f'

def setup_inputs(seed: int=0):
    np.random.seed(seed)
    _w = jnp.asarray

    def _rec_inputs():
        import jax
        import jax.numpy as jnp
        _tk = jax.random.key(seed)
        ids = jnp.stack([jax.random.randint(jax.random.fold_in(_tk, 200 + f), (2048,), 0, v, jnp.int32) for f, v in enumerate([12500, 1250, 1000, 1250, 12500, 125000, 1250, 12500, 12500, 12500, 1000, 1250, 1250, 1250, 1250, 1000, 1000, 12500, 1250, 12500, 12500, 1000, 1250, 1250, 1250, 1000])], axis=1)
        tbl_0 = 0.05 * jax.random.normal(jax.random.fold_in(_tk, 500 + 0), (12500, 128), jnp.float32)
        tbl_1 = 0.05 * jax.random.normal(jax.random.fold_in(_tk, 500 + 1), (1250, 128), jnp.float32)
        tbl_2 = 0.05 * jax.random.normal(jax.random.fold_in(_tk, 500 + 2), (1000, 128), jnp.float32)
        tbl_3 = 0.05 * jax.random.normal(jax.random.fold_in(_tk, 500 + 3), (1250, 128), jnp.float32)
        tbl_4 = 0.05 * jax.random.normal(jax.random.fold_in(_tk, 500 + 4), (12500, 128), jnp.float32)
        tbl_5 = 0.05 * jax.random.normal(jax.random.fold_in(_tk, 500 + 5), (125000, 128), jnp.float32)
        tbl_6 = 0.05 * jax.random.normal(jax.random.fold_in(_tk, 500 + 6), (1250, 128), jnp.float32)
        tbl_7 = 0.05 * jax.random.normal(jax.random.fold_in(_tk, 500 + 7), (12500, 128), jnp.float32)
        tbl_8 = 0.05 * jax.random.normal(jax.random.fold_in(_tk, 500 + 8), (12500, 128), jnp.float32)
        tbl_9 = 0.05 * jax.random.normal(jax.random.fold_in(_tk, 500 + 9), (12500, 128), jnp.float32)
        tbl_10 = 0.05 * jax.random.normal(jax.random.fold_in(_tk, 500 + 10), (1000, 128), jnp.float32)
        tbl_11 = 0.05 * jax.random.normal(jax.random.fold_in(_tk, 500 + 11), (1250, 128), jnp.float32)
        tbl_12 = 0.05 * jax.random.normal(jax.random.fold_in(_tk, 500 + 12), (1250, 128), jnp.float32)
        tbl_13 = 0.05 * jax.random.normal(jax.random.fold_in(_tk, 500 + 13), (1250, 128), jnp.float32)
        tbl_14 = 0.05 * jax.random.normal(jax.random.fold_in(_tk, 500 + 14), (1250, 128), jnp.float32)
        tbl_15 = 0.05 * jax.random.normal(jax.random.fold_in(_tk, 500 + 15), (1000, 128), jnp.float32)
        tbl_16 = 0.05 * jax.random.normal(jax.random.fold_in(_tk, 500 + 16), (1000, 128), jnp.float32)
        tbl_17 = 0.05 * jax.random.normal(jax.random.fold_in(_tk, 500 + 17), (12500, 128), jnp.float32)
        tbl_18 = 0.05 * jax.random.normal(jax.random.fold_in(_tk, 500 + 18), (1250, 128), jnp.float32)
        tbl_19 = 0.05 * jax.random.normal(jax.random.fold_in(_tk, 500 + 19), (12500, 128), jnp.float32)
        tbl_20 = 0.05 * jax.random.normal(jax.random.fold_in(_tk, 500 + 20), (12500, 128), jnp.float32)
        tbl_21 = 0.05 * jax.random.normal(jax.random.fold_in(_tk, 500 + 21), (1000, 128), jnp.float32)
        tbl_22 = 0.05 * jax.random.normal(jax.random.fold_in(_tk, 500 + 22), (1250, 128), jnp.float32)
        tbl_23 = 0.05 * jax.random.normal(jax.random.fold_in(_tk, 500 + 23), (1250, 128), jnp.float32)
        tbl_24 = 0.05 * jax.random.normal(jax.random.fold_in(_tk, 500 + 24), (1250, 128), jnp.float32)
        tbl_25 = 0.05 * jax.random.normal(jax.random.fold_in(_tk, 500 + 25), (1000, 128), jnp.float32)
        _rk = jax.random.fold_in(_tk, 7)
        r_dense_features = -0.000520686 + 1.00062 * jax.random.normal(jax.random.fold_in(_rk, 101), (2048, 128), jnp.float32)
        W_top1 = 0.0405887 * jax.random.normal(jax.random.fold_in(_tk, 801), (607, 512), jnp.float32)
        W_top2 = 0.0441942 * jax.random.normal(jax.random.fold_in(_tk, 802), (512, 256), jnp.float32)
        W_top3 = 0.0625 * jax.random.normal(jax.random.fold_in(_tk, 803), (256, 1), jnp.float32)
        b_top1 = jnp.zeros((512,), jnp.float32)
        b_top2 = jnp.zeros((256,), jnp.float32)
        return (r_dense_features, ids, tbl_0, tbl_1, tbl_2, tbl_3, tbl_4, tbl_5, tbl_6, tbl_7, tbl_8, tbl_9, tbl_10, tbl_11, tbl_12, tbl_13, tbl_14, tbl_15, tbl_16, tbl_17, tbl_18, tbl_19, tbl_20, tbl_21, tbl_22, tbl_23, tbl_24, tbl_25, W_top1, b_top1, W_top2, b_top2, W_top3)
    r_dense_features, ids, tbl_0, tbl_1, tbl_2, tbl_3, tbl_4, tbl_5, tbl_6, tbl_7, tbl_8, tbl_9, tbl_10, tbl_11, tbl_12, tbl_13, tbl_14, tbl_15, tbl_16, tbl_17, tbl_18, tbl_19, tbl_20, tbl_21, tbl_22, tbl_23, tbl_24, tbl_25, W_top1, b_top1, W_top2, b_top2, W_top3 = _rec_inputs()

    def _L0_rec_setup():
        import jax, jax.numpy as jnp
        import numpy as np
        B, F, D = (2048, 26, 128)
        key = jax.random.key(seed)
        k1, k2 = jax.random.split(key)
        dense_features = jax.random.normal(k1, (B, D), dtype=jnp.float32)
        sparse_features = jax.random.normal(k2, (B, F, D), dtype=jnp.float32)
        return {'dense_features': dense_features, 'sparse_features': sparse_features}
    _L0_rec_all = _L0_rec_setup()
    _L0_rec_in = {k: v for k, v in _L0_rec_all.items() if k in ()}
    del _L0_rec_all
    return {'r_dense_features': r_dense_features, 'ids': ids, 'tbl_0': tbl_0, 'tbl_1': tbl_1, 'tbl_2': tbl_2, 'tbl_3': tbl_3, 'tbl_4': tbl_4, 'tbl_5': tbl_5, 'tbl_6': tbl_6, 'tbl_7': tbl_7, 'tbl_8': tbl_8, 'tbl_9': tbl_9, 'tbl_10': tbl_10, 'tbl_11': tbl_11, 'tbl_12': tbl_12, 'tbl_13': tbl_13, 'tbl_14': tbl_14, 'tbl_15': tbl_15, 'tbl_16': tbl_16, 'tbl_17': tbl_17, 'tbl_18': tbl_18, 'tbl_19': tbl_19, 'tbl_20': tbl_20, 'tbl_21': tbl_21, 'tbl_22': tbl_22, 'tbl_23': tbl_23, 'tbl_24': tbl_24, 'tbl_25': tbl_25, 'W_top1': W_top1, 'b_top1': b_top1, 'W_top2': W_top2, 'b_top2': b_top2, 'W_top3': W_top3}

def reference(r_dense_features, ids, tbl_0, tbl_1, tbl_2, tbl_3, tbl_4, tbl_5, tbl_6, tbl_7, tbl_8, tbl_9, tbl_10, tbl_11, tbl_12, tbl_13, tbl_14, tbl_15, tbl_16, tbl_17, tbl_18, tbl_19, tbl_20, tbl_21, tbl_22, tbl_23, tbl_24, tbl_25, W_top1, b_top1, W_top2, b_top2, W_top3):
    import jax
    import jax.numpy as jnp

    def _L0_rec_ref(dense_features, sparse_features):
        import jax, jax.numpy as jnp
        import numpy as np
        B, F, D = (2048, 26, 128)
        combined = jnp.concatenate([dense_features[:, None, :], sparse_features], axis=1)
        interactions = jnp.einsum('bfd,bgd->bfg', combined, combined)
        iu0, iu1 = np.triu_indices(F + 1, k=1)
        interactions_flat = interactions[:, iu0, iu1]
        return jnp.concatenate([dense_features, interactions_flat], axis=1)
    e = jnp.stack([tbl_0[ids[:, 0]], tbl_1[ids[:, 1]], tbl_2[ids[:, 2]], tbl_3[ids[:, 3]], tbl_4[ids[:, 4]], tbl_5[ids[:, 5]], tbl_6[ids[:, 6]], tbl_7[ids[:, 7]], tbl_8[ids[:, 8]], tbl_9[ids[:, 9]], tbl_10[ids[:, 10]], tbl_11[ids[:, 11]], tbl_12[ids[:, 12]], tbl_13[ids[:, 13]], tbl_14[ids[:, 14]], tbl_15[ids[:, 15]], tbl_16[ids[:, 16]], tbl_17[ids[:, 17]], tbl_18[ids[:, 18]], tbl_19[ids[:, 19]], tbl_20[ids[:, 20]], tbl_21[ids[:, 21]], tbl_22[ids[:, 22]], tbl_23[ids[:, 23]], tbl_24[ids[:, 24]], tbl_25[ids[:, 25]]], axis=1)
    z = _L0_rec_ref(r_dense_features, e)
    z = z.reshape(z.shape[0], -1)
    h = jnp.concatenate([z, r_dense_features], axis=1)
    h = jnp.maximum(h @ W_top1 + b_top1, 0.0)
    h = jnp.maximum(h @ W_top2 + b_top2, 0.0)
    y = h @ W_top3
    return y

_drawn_inputs = setup_inputs


def setup_inputs(seed=0):
    import zlib

    import numpy as np

    out = dict(_drawn_inputs(seed))
    spreads = {'b_top1': (0.0, 0.1), 'b_top2': (0.0, 0.1)}
    factors = {}
    for name, (base, spread) in spreads.items():
        noise = np.random.default_rng([zlib.crc32(name.encode()), seed]).standard_normal(out[name].shape)
        drawn = base * np.exp(spread * noise) if base else spread * noise
        out[name] = jnp.asarray(drawn.astype(out[name].dtype))
    for name, factor in factors.items():
        out[name] = (out[name] * factor).astype(out[name].dtype)
    return out
```

```python
from contextlib import ExitStack

import numpy as np

import concourse.bass as bass
from concourse import mybir

F32 = mybir.dt.float32
BF16 = mybir.dt.bfloat16
I32 = mybir.dt.int32
ALU = mybir.AluOpType
ACT = mybir.ActivationFunctionType

SUMMED = (2, 10, 15, 16, 21, 25)
P = 128
D = 128
QUAD = 32
GROUP = 4
TILE = 128
HALVES = 2
STEP = TILE * HALVES
SLOTS = 2
PARTS = 3


def dlrm_kernel(nc, ins, out):
    n_samples, n_tables = ins["ids"].shape
    feats = n_tables + 1
    cols = feats - 1
    n_pairs = feats * cols // 2
    steps = n_samples // STEP
    rounds = steps // SLOTS
    tables = [ins[f"tbl_{t}"] for t in range(n_tables)]
    hid1, hid2 = ins["W_top2"].shape
    m1, m2 = hid1 // P, hid2 // P
    z_chunks = [(c, min(P, n_pairs - c)) for c in range(0, n_pairs, P)]

    summed = list(SUMMED)
    K = len(summed)
    rows_p = 125
    chunks = [tables[t].shape[0] // rows_p for t in summed]
    assert all(tables[t].shape[0] == rows_p * c for t, c in zip(summed, chunks))
    chunk_at = [sum(chunks[:j]) for j in range(K)]
    max_chunks = max(chunks)
    gathered = [t for t in range(n_tables) if t not in summed]
    NG = len(gathered)
    rows = [(0, 0)] + [(1 + i, 1 + t) for i, t in enumerate(gathered)]
    batches = []
    for place, feat in rows:
        if batches and len(batches[-1]) < 4 and batches[-1][-1][1] == feat - 1:
            batches[-1].append((place, feat))
        else:
            batches.append([(place, feat)])
    NB = len(batches)
    batches_of = [(NB + 1) // 2, NB // 2]
    tables_of = [(K + 1) // 2, K // 2]
    GPT = 8
    NGR = TILE // GROUP // GPT
    MLP_USES = [m1 // 2 + m2 // 2 + 1, m1 // 2 + m2 // 2]

    pair_moves = []
    base = 0
    for f in range(cols):
        g, n = f + 1, cols - f
        while n:
            c, r = divmod(base, P)
            m = min(n, P - r)
            pair_moves.append((f, g, m, c, r))
            g, n, base = g + m, n - m, base + m
    PAIRS_DONE = 16 * len(pair_moves)

    with ExitStack() as ctx:
        def sb(name, shape, dt=F32):
            return ctx.enter_context(nc.sbuf_tensor(name, shape, dt))

        def ps(name, shape):
            return ctx.enter_context(nc.psum_tensor(name, shape, F32))

        def sem(name):
            return ctx.enter_context(nc.semaphore(name))

        def sems(name, n):
            return [sem(f"{name}{i}") for i in range(n)]

        ident = sb("ident", [P, P])
        row_number = {c: sb(f"row_number{c}", [rows_p, c]) for c in sorted(set(chunks))}
        w1_pairs = sb("w1_pairs", [P, len(z_chunks), hid1])
        w1_dense = sb("w1_dense", [P, hid1])
        w2 = sb("w2", [P, m1, hid2])
        w3 = sb("w3", [P, m2])
        b1 = sb("b1", [P, m1])
        b2 = sb("b2", [P, m2])
        parts = [sb(f"parts{q}", [rows_p, sum(chunks), D], BF16) for q in range(PARTS)]
        ids = [sb(f"ids{s}", [P, HALVES, n_tables], I32) for s in range(SLOTS)]
        ids_wide = sb("ids_wide", [P, K, STEP], I32)
        rows_in = [sb(f"rows_in{s}", [P, 1 + NG, D]) for s in range(SLOTS * HALVES)]
        onehot = [sb(f"onehot{q}", [rows_p, max_chunks, STEP], BF16) for q in range(2)]
        XT = [sb(f"XT{s}", [P, STEP, QUAD]) for s in range(SLOTS)]
        dots_room = sb("dots_room", [P, max(cols * STEP, sum(chunks) * D)])
        dots = dots_room[0:feats, 0:cols * STEP].rearrange("g (f b) -> g f b", f=cols)
        zT = sb("zT", [P, len(z_chunks), STEP])
        h1 = sb("h1", [P, m1, STEP])
        w1_dense_again = h1[:, :, :].rearrange("p m b -> p (m b)")[:, 0:hid1]
        h2 = sb("h2", [P, m2, STEP])
        y = [sb(f"y{s}", [1, STEP]) for s in range(SLOTS)]

        turned = [ps(f"turned{q}", [P, 4, TILE]) for q in range(2)]
        grams = [ps(f"grams{q}", [P, GPT, P]) for q in range(2)]
        sums = [ps(f"sums{q}", [P, STEP]) for q in range(2)]

        ident_made = sem("ident_made")
        rows_numbered = sem("rows_numbered")
        weights_in = sem("weights_in")
        tables_in = sems("tables_in", K)
        high_cut = sem("high_cut")
        rest_cut = sem("rest_cut")
        mid_cut = sem("mid_cut")
        low_cut = sem("low_cut")
        dense_merged = sem("dense_merged")
        pad_set = sem("pad_set")
        ids_in = sems("ids_in", SLOTS)
        ids_wide_in = sem("ids_wide_in")
        dense_in = sems("dense_in", SLOTS * HALVES)
        rows_gathered = sems("rows_gathered", SLOTS * HALVES)
        rows_free = sems("rows_free", SLOTS * HALVES)
        gather_go = sem("gather_go")
        onehot_made = sem("onehot_made")
        summed_up = sems("summed_up", 2)
        sums_out = sems("sums_out", 2)
        tiles_turned = sems("tiles_turned", 2)
        turned_out = sems("turned_out", 2)
        dots_summed = sems("dots_summed", 2)
        dots_out = sems("dots_out", 2)
        pairs_moved = sem("pairs_moved")
        y_stored = sems("y_stored", SLOTS)

        block = ctx.enter_context(nc.Block())

        def stage_of(j):
            return dots_room[0:rows_p, chunk_at[j] * D:(chunk_at[j] + chunks[j]) * D]

        def part_of(part, j):
            return parts[part][:, chunk_at[j]:chunk_at[j] + chunks[j], :].rearrange("p c d -> p (c d)")

        def before_onehot(q, step, first=False):
            return 0 if first else (tables_of[q] + MLP_USES[q]) * step - MLP_USES[q]

        def before_mlp(q, step, more):
            return (tables_of[q] + MLP_USES[q]) * step + tables_of[q] * (2 if more else 1)

        @block.sync
        def _(sp):
            def load_step(step, s, r):
                sp.dma_start(ids[s][:, :, :],
                             ins["ids"][bass.ds(step * STEP, STEP), :].rearrange("(h p) f -> p h f", p=P)
                             ).then_inc(ids_in[s], 16)
                for h in range(HALVES):
                    k = HALVES * s + h
                    sp.wait_ge(rows_free[k], r + 1)
                    sp.dma_start(rows_in[k][:, 0, :],
                                 ins["r_dense_features"][bass.ds(step * STEP + h * TILE, TILE), :]
                                 ).then_inc(dense_in[k], 16)

            def load_ids_wide(step):
                for j in range(K):
                    sp.dma_start(ids_wide[:, j, :],
                                 ins["ids_by_table"][summed[j]:summed[j] + 1, bass.ds(step * STEP, STEP)]
                                 .broadcast_to([P, STEP])).then_inc(ids_wide_in, 16)

            sp.sem_inc(pairs_moved, 16)
            for s in range(SLOTS):
                sp.sem_inc(y_stored[s], 16)
            load_step(0, 0, 0)
            load_ids_wide(0)
            for j in range(K):
                sp.dma_start(stage_of(j), tables[summed[j]].rearrange("(p c) d -> p (c d)", p=rows_p)
                             ).then_inc(tables_in[j], 16)
            for c, (at, n) in enumerate(z_chunks):
                sp.dma_start(w1_pairs[0:n, c, :], ins["W_top1"][D + at:D + at + n, :]).then_inc(weights_in, 16)
            sp.dma_start(w1_dense[:, :], ins["W_top1"][0:D, :]).then_inc(weights_in, 16)
            sp.dma_start(w1_dense_again[:, :], ins["W_top1"][D + n_pairs:, :]).then_inc(weights_in, 16)
            sp.dma_start(w2[:, :, :], ins["W_top2"].rearrange("(c p) n -> p c n", p=P)).then_inc(weights_in, 16)
            with nc.allow_non_contiguous_dma(reason="896 single numbers, once"):
                sp.dma_start(w3[:, :], ins["W_top3"].rearrange("(c p) o -> p (c o)", p=P)).then_inc(weights_in, 16)
                sp.dma_start(b1[:, :], ins["b_top1"].rearrange("(c p) -> p c", p=P)).then_inc(weights_in, 16)
                sp.dma_start(b2[:, :], ins["b_top2"].rearrange("(c p) -> p c", p=P)).then_inc(weights_in, 16)
            load_step(1, 1, 0)
            sp.wait_ge(onehot_made, K)
            load_ids_wide(1)

            def body(step, r, s, load_ahead, more):
                for q in range(2):
                    sp.wait_ge(dots_out[q], 1 + HALVES * NGR // 2 * (step + 1))
                for f, g, n, c, row in pair_moves:
                    sp.dma_start(zT[row:row + n, c, :], dots[g:g + n, f, :]).then_inc(pairs_moved, 16)
                if load_ahead:
                    for h in range(HALVES):
                        sp.wait_ge(rows_gathered[HALVES * s + h], 16 * NG * (r + 1))
                    load_step(step + SLOTS, s, r + 1)
                    sp.wait_ge(onehot_made, K * (step + 2))
                    load_ids_wide(step + 2)
                sp.wait_ge(sums_out[0], 1 + before_mlp(0, step, more) + MLP_USES[0])
                sp.dma_start(out[bass.ds(step * STEP, STEP), :].rearrange("b o -> o b"), y[s][:, :]
                             ).then_inc(y_stored[s], 16)

            with sp.Fori(0, rounds - 1) as r:
                for s in range(SLOTS):
                    body(r * SLOTS + s, r, s, True, True)
            for s in range(SLOTS):
                body((rounds - 1) * SLOTS + s, rounds - 1, s, False, s < SLOTS - 1)
            for s in range(SLOTS):
                sp.wait_ge(y_stored[s], 16 * (rounds + 1))

        @block.gpsimd
        def _(pool):
            def gather(r, s, h):
                k = HALVES * s + h
                pool.wait_ge(rows_free[k], r + 1)
                pool.sem_inc(gather_go, 1)
                for i, t in enumerate(gathered):
                    pool.indirect_dma_start(
                        out=rows_in[k][:, 1 + i, :], out_offset=None, in_=tables[t],
                        in_offset=bass.IndirectOffsetOnAxis(ap=ids[s][:, h, t:t + 1], axis=0)
                    ).then_inc(rows_gathered[k], 16)

            nc.gpsimd.memset(ident[:, :], 0.0).then_inc(ident_made, 1)
            for n, col in row_number.items():
                nc.gpsimd.iota(col[:, :], [[1, n]], base=0, channel_multiplier=n,
                               allow_small_or_imprecise_dtypes=True).then_inc(rows_numbered, 1)
            pool.wait_ge(ident_made, 1)
            nc.gpsimd.affine_select(out=ident[:, :], in_=ident[:, :], compare_op=ALU.not_equal, fill=1.0,
                                    base=0, pattern=[[-1, P]], channel_multiplier=1).then_inc(ident_made, 1)
            with pool.Fori(0, rounds) as r:
                for s in range(SLOTS):
                    pool.wait_ge(ids_in[s], 16 * (r + 1))
                    pool.sem_inc(gather_go, 1)
                    for h in range(HALVES):
                        gather(r, s, h)

        def copy_turned(eng, copy, q, step, s, h):
            for i in range(q, NB, 2):
                b = batches[i]
                eng.wait_ge(tiles_turned[q], batches_of[q] * (step * HALVES + h) + i // 2 + 1)
                f = b[0][1]
                copy(XT[s][:, h * TILE:(h + 1) * TILE, f:f + len(b)],
                     turned[q][:, 0:len(b), :].rearrange("p f b -> p b f")).then_inc(turned_out[q], 1)

        def copy_dots(eng, copy, q, step, s, h):
            if h == 0:
                eng.wait_ge(pairs_moved, 16 + PAIRS_DONE * step)
            for i in range(q, NGR, 2):
                eng.wait_ge(dots_summed[q], NGR // 2 * (step * HALVES + h) + i // 2 + 1)
                for j in range(GROUP):
                    at = h * TILE + i * GPT * GROUP
                    last = copy(dots[:, :, at + j:at + GPT * GROUP:GROUP],
                                grams[q][QUAD * j:QUAD * j + feats, :, j * cols:(j + 1) * cols]
                                .rearrange("p t f -> p f t"))
                last.then_inc(dots_out[q], 1)

        def copy_onehot(eng, copy, q, step, s, j, first=False):
            eng.wait_ge(summed_up[q], before_onehot(q, step, first) + j // 2 + 1)
            copy(XT[s][:, :, 1 + summed[j]], sums[q][:, :]).then_inc(sums_out[q], 1)

        @block.scalar
        def _(act):
            def copy(o, i):
                return nc.scalar.copy(o, i)

            for j in range(K):
                act.wait_ge(tables_in[j], 16)
                nc.scalar.copy(part_of(0, j), stage_of(j)).then_inc(high_cut, 1)
                if j:
                    act.wait_ge(rest_cut, j)
                    nc.scalar.copy(part_of(1, j - 1), stage_of(j - 1)).then_inc(mid_cut, 1)
            act.wait_ge(rest_cut, K)
            nc.scalar.copy(part_of(1, K - 1), stage_of(K - 1)).then_inc(mid_cut, 1)
            for j in range(0, K, 2):
                copy_onehot(act, copy, 0, 0, 0, j, True)
            act.wait_ge(weights_in, 16 * 9)

            def body(step, r, s, more):
                for h in range(HALVES):
                    copy_turned(act, copy, 0, step, s, h)
                    copy_dots(act, copy, 0, step, s, h)
                if more:
                    for j in range(0, K, 2):
                        copy_onehot(act, copy, 0, step + 1, 1 - s, j)
                used = 0
                for h, b, n in ((h1, b1, m1), (h2, b2, m2)):
                    for m in range(0, n, 2):
                        used += 1
                        act.wait_ge(summed_up[0], before_mlp(0, step, more) + used)
                        nc.scalar.activation(h[:, m, :], sums[0][:, :], ACT.Relu,
                                             bias=b[:, m:m + 1]).then_inc(sums_out[0], 1)
                act.wait_ge(summed_up[0], before_mlp(0, step, more) + MLP_USES[0])
                act.wait_ge(y_stored[s], 16 * (r + 1))
                copy(y[s][:, :], sums[0][0:1, :]).then_inc(sums_out[0], 1)

            with act.Fori(0, rounds - 1) as r:
                for s in range(SLOTS):
                    body(r * SLOTS + s, r, s, True)
            for s in range(SLOTS):
                body((rounds - 1) * SLOTS + s, rounds - 1, s, s < SLOTS - 1)

        @block.vector
        def _(dve):
            def copy(o, i):
                return nc.vector.tensor_copy(o, i)

            def make_onehot(step, r, s, j, first=False):
                if j < 2:
                    dve.wait_ge(ids_wide_in, 16 * K * (step + 1))
                if not (first and j < 2):
                    dve.wait_ge(summed_up[j % 2], before_onehot(j % 2, step, first) + j // 2)
                col = row_number[chunks[j]]
                for c in range(chunks[j]):
                    last = nc.vector.tensor_scalar(onehot[j % 2][:, c, :], ids_wide[0:rows_p, j, :],
                                                   col[:, c:c + 1], None, ALU.is_equal)
                last.then_inc(onehot_made, 1)

            def onehot_rest(step, r, s, first=False):
                for j in range(K):
                    if j % 2:
                        copy_onehot(dve, copy, 1, step, s, j, first)
                    if j + 2 < K:
                        make_onehot(step, r, s, j + 2, first)

            for s in range(SLOTS):
                last = nc.vector.memset(XT[s][:, :, feats:], 0.0)
            last.then_inc(pad_set, 1)
            dve.wait_ge(rows_numbered, len(row_number))
            for j in range(2):
                make_onehot(0, 0, 0, j, True)
            for j in range(K):
                dve.wait_ge(high_cut, j + 1)
                nc.vector.tensor_tensor(stage_of(j), stage_of(j), part_of(0, j), ALU.subtract
                                        ).then_inc(rest_cut, 1)
                if j:
                    dve.wait_ge(mid_cut, j)
                    nc.vector.tensor_tensor(part_of(2, j - 1), stage_of(j - 1), part_of(1, j - 1),
                                            ALU.subtract).then_inc(low_cut, 1)
            dve.wait_ge(mid_cut, K)
            nc.vector.tensor_tensor(part_of(2, K - 1), stage_of(K - 1), part_of(1, K - 1),
                                    ALU.subtract).then_inc(low_cut, 1)
            dve.wait_ge(weights_in, 16 * 9)
            nc.vector.tensor_tensor(w1_dense[:, :], w1_dense[:, :], w1_dense_again[:, :], ALU.add
                                    ).then_inc(dense_merged, 1)
            onehot_rest(0, 0, 0, True)

            def body(step, r, s, more, ahead):
                for h in range(HALVES):
                    copy_turned(dve, copy, 1, step, s, h)
                    if more and h == 0:
                        for j in range(2):
                            make_onehot(step + 1, ahead, 1 - s, j)
                    copy_dots(dve, copy, 1, step, s, h)
                if more:
                    onehot_rest(step + 1, ahead, 1 - s)
                used = 0
                for h, b, n in ((h1, b1, m1), (h2, b2, m2)):
                    for m in range(1, n, 2):
                        used += 1
                        dve.wait_ge(summed_up[1], before_mlp(1, step, more) + used)
                        nc.vector.tensor_scalar(h[:, m, :], sums[1][:, :], b[:, m:m + 1], 0.0,
                                                ALU.add, ALU.max).then_inc(sums_out[1], 1)

            with dve.Fori(0, rounds - 1) as r:
                for s in range(SLOTS):
                    body(r * SLOTS + s, r, s, True, r + (s == SLOTS - 1))
            for s in range(SLOTS):
                body((rounds - 1) * SLOTS + s, rounds - 1, s, s < SLOTS - 1, rounds - 1)

        @block.tensor
        def _(pe):
            def onehot_sums(step, s, first=False):
                for j in range(K):
                    q = j % 2
                    if first:
                        pe.wait_ge(low_cut, j + 1)
                    pe.wait_ge(onehot_made, K * step + j + 1)
                    pe.wait_ge(sums_out[q], before_onehot(q, step, first) + j // 2 + 1)
                    for c in range(chunks[j]):
                        for part in range(PARTS):
                            last = nc.tensor.matmul(sums[q][:, :], parts[part][:, chunk_at[j] + c, :],
                                                    onehot[q][:, c, :], start=(c == 0 and part == 0),
                                                    stop=(c == chunks[j] - 1 and part == PARTS - 1))
                    last.then_inc(summed_up[q], 1)

            def transposes(step, r, s, h):
                k = HALVES * s + h
                pe.wait_ge(dense_in[k], 16 * (r + 1))
                pe.wait_ge(rows_gathered[k], 16 * NG * (r + 1))
                for i, b in enumerate(batches):
                    q = i % 2
                    pe.wait_ge(turned_out[q], batches_of[q] * (step * HALVES + h) + i // 2 + 1)
                    for n, (place, _) in enumerate(b):
                        last = nc.tensor.transpose(turned[q][:, n, :], rows_in[k][:, place, :], ident[:, :])
                    last.then_inc(tiles_turned[q], 1)

            def dot_products(step, s, h):
                for q in range(2):
                    pe.wait_ge(turned_out[q], 1 + batches_of[q] * (step * HALVES + h + 1))
                    if h == 0:
                        pe.wait_ge(sums_out[q], 1 + (tables_of[q] + MLP_USES[q]) * step + tables_of[q])
                for i in range(NGR):
                    q = i % 2
                    pe.wait_ge(dots_out[q], NGR // 2 * (step * HALVES + h) + i // 2 + 1)
                    for t in range(GPT):
                        b0 = h * TILE + (i * GPT + t) * GROUP
                        four = XT[s][:, b0:b0 + GROUP, :]
                        last = nc.tensor.matmul(grams[q][:, t, 0:GROUP * cols].rearrange("p (b f) -> p b f", f=cols),
                                                four.rearrange("p b f -> p (b f)"), four[:, :, 0:cols], start=True, stop=True)
                        if i == t == 0:
                            last.then_inc(rows_free[HALVES * s + h], 1)
                    last.then_inc(dots_summed[q], 1)

            def perceptron(step, s, more):
                pe.wait_ge(pairs_moved, 16 + PAIRS_DONE * (step + 1))
                dense = XT[s][:, :, 0]
                used = [0, 0]

                def psum(q):
                    used[q] += 1
                    pe.wait_ge(sums_out[q], before_mlp(q, step, more) + used[q])
                    return sums[q][:, :]

                for m in range(m1):
                    acc = psum(m % 2)
                    nc.tensor.matmul(acc, w1_dense[:, m * P:(m + 1) * P], dense, start=True, stop=False)
                    for c, (_, n) in enumerate(z_chunks):
                        last = nc.tensor.matmul(acc, w1_pairs[0:n, c, m * P:(m + 1) * P], zT[0:n, c, :],
                                                start=False, stop=(c == len(z_chunks) - 1))
                    last.then_inc(summed_up[m % 2], 1)
                for q in range(2):
                    pe.wait_ge(sums_out[q], before_mlp(q, step, more) + m1 // 2 + 1)
                for m in range(m2):
                    acc = psum(m % 2)
                    for c in range(m1):
                        last = nc.tensor.matmul(acc, w2[:, c, m * P:(m + 1) * P], h1[:, c, :],
                                                start=(c == 0), stop=(c == m1 - 1))
                    last.then_inc(summed_up[m % 2], 1)
                for q in range(2):
                    pe.wait_ge(sums_out[q], before_mlp(q, step, more) + m1 // 2 + m2 // 2 + 1)
                for c in range(m2):
                    last = nc.tensor.matmul(sums[0][0:1, :], w3[:, c:c + 1], h2[:, c, :],
                                            start=(c == 0), stop=(c == m2 - 1))
                last.then_inc(summed_up[0], 1)

            for s in [*rows_free, *turned_out, *dots_out, *sums_out]:
                pe.sem_inc(s, 1)
            pe.wait_ge(ident_made, 2)
            pe.wait_ge(pad_set, 1)
            onehot_sums(0, 0, True)
            pe.wait_ge(weights_in, 16 * 9)
            pe.wait_ge(dense_merged, 1)

            def body(step, r, s, more):
                for h in range(HALVES):
                    transposes(step, r, s, h)
                    dot_products(step, s, h)
                if more:
                    onehot_sums(step + 1, 1 - s)
                perceptron(step, s, more)

            with pe.Fori(0, rounds - 1) as r:
                for s in range(SLOTS):
                    body(r * SLOTS + s, r, s, True)
            for s in range(SLOTS):
                body((rounds - 1) * SLOTS + s, rounds - 1, s, s < SLOTS - 1)


def kernel(**inputs):
    import concourse.bacc as bacc
    from concourse.bass_utils import run_bass_kernel_spmd

    nc = bacc.Bacc("TRN2", target_bir_lowering=False, num_devices=1)
    given = dict(inputs, ids_by_table=np.asarray(inputs["ids"]).T)
    arrays, ins = {}, {}
    for name, value in given.items():
        a = np.ascontiguousarray(value)
        arrays[f"in_{name}"] = a
        ins[name] = nc.dram_tensor(f"in_{name}", a.shape, mybir.dt.from_np(a.dtype), kind="ExternalInput").ap()
    n = arrays["in_ids"].shape[0]
    out = nc.dram_tensor("out_y", (n, 1), F32, kind="ExternalOutput").ap()
    dlrm_kernel(nc, ins, out)
    return run_bass_kernel_spmd(nc, [arrays], core_ids=[0]).results[0]["out_y"]
```

```python
from contextlib import ExitStack

import numpy as np

import concourse.bass as bass
from concourse import mybir

F32 = mybir.dt.float32
F32R = mybir.dt.float32r
I32 = mybir.dt.int32
ALU = mybir.AluOpType
ACT = mybir.ActivationFunctionType

SUMMED = (2, 10, 15, 16, 21, 25)
P = 128
D = 128
QUAD = 32
GROUP = 4
TILE = 128
HALVES = 2
STEP = TILE * HALVES
SLOTS = 2
PARTS = 2


def dlrm_kernel(nc, ins, out):
    n_samples, n_tables = ins["ids"].shape
    feats = n_tables + 1
    cols = feats - 1
    n_pairs = feats * cols // 2
    steps = n_samples // STEP
    turns = (steps - 2) // SLOTS
    tables = [ins[f"tbl_{t}"] for t in range(n_tables)]
    hid1, hid2 = ins["W_top2"].shape
    m1, m2 = hid1 // P, hid2 // P

    summed = list(SUMMED)
    K = len(summed)
    rows_p = 125
    chunks = [tables[t].shape[0] // rows_p for t in summed]
    assert all(tables[t].shape[0] == rows_p * c for t, c in zip(summed, chunks))
    chunk_at = [sum(chunks[:j]) for j in range(K)]
    max_chunks = max(chunks)
    gathered = [t for t in range(n_tables) if t not in summed]
    NG = len(gathered)
    rows = [(0, 0)] + [(1 + i, 1 + t) for i, t in enumerate(gathered)]
    batches = []
    for place, feat in rows:
        if batches and len(batches[-1]) < 4 and batches[-1][-1][1] == feat - 1:
            batches[-1].append((place, feat))
        else:
            batches.append([(place, feat)])
    NB = len(batches)
    batches_of = [(NB + 1) // 2, NB // 2]
    tables_of = [(K + 1) // 2, K // 2]
    GPT = 8
    NGR = TILE // GROUP // GPT
    MLP_USES = [m1 // 2 + m2 // 2 + 1, m1 // 2 + m2 // 2]

    base_of = [sum(cols - e for e in range(f)) for f in range(cols)]
    ZC = 4
    native = ZC * (P // QUAD)
    folded = cols - native
    fold_at = [((native - 1 - i) // 4, QUAD * ((native - 1 - i) % 4), folded - i) for i in range(folded)]
    assert all(n <= native - i for i, (_, _, n) in enumerate(fold_at))
    PAIRS_DONE = 16 * folded

    with ExitStack() as ctx:
        def sb(name, shape, dt=F32):
            return ctx.enter_context(nc.sbuf_tensor(name, shape, dt))

        def ps(name, shape):
            return ctx.enter_context(nc.psum_tensor(name, shape, F32))

        def sem(name):
            return ctx.enter_context(nc.semaphore(name))

        def sems(name, n):
            return [sem(f"{name}{i}") for i in range(n)]

        ident = sb("ident", [P, P])
        row_number = {c: sb(f"row_number{c}", [rows_p, c]) for c in sorted(set(chunks))}
        w1_pairs = sb("w1_pairs", [P, ZC, hid1])
        w1_dense = sb("w1_dense", [P, hid1])
        w2 = sb("w2", [P, m1, hid2])
        w3 = sb("w3", [P, m2])
        b1 = sb("b1", [P, m1])
        b2 = sb("b2", [P, m2])
        parts = [sb(f"parts{q}", [rows_p, sum(chunks), D], F32R) for q in range(PARTS)]
        ids = [sb(f"ids{s}", [P, HALVES, n_tables], I32) for s in range(SLOTS)]
        ids_wide = sb("ids_wide", [P, K, STEP], I32)
        rows_in = [sb(f"rows_in{s}", [P, 1 + NG, D]) for s in range(SLOTS * HALVES)]
        onehot = [sb(f"onehot{q}", [rows_p, max_chunks, STEP], F32R) for q in range(2)]
        XT = sb("XT", [P, STEP, QUAD])
        dense_T = [sb(f"dense_T{s}", [P, STEP]) for s in range(SLOTS)]
        z = sb("z", [P, ZC, STEP])
        short = sb("short", [feats, folded, STEP])
        h1 = sb("h1", [P, m1, STEP])
        w1_dense_again = h1[:, :, :].rearrange("p m b -> p (m b)")[:, 0:hid1]
        h2 = sb("h2", [P, m2, STEP])
        y = [sb(f"y{s}", [1, STEP]) for s in range(SLOTS)]

        turned = [ps(f"turned{q}", [P, 4, TILE]) for q in range(2)]
        grams = [ps(f"grams{q}", [P, GPT, P]) for q in range(2)]
        sums = [ps(f"sums{q}", [P, STEP]) for q in range(2)]

        ident_made = sem("ident_made")
        rows_numbered = sem("rows_numbered")
        weights_in = sem("weights_in")
        tables_in = sems("tables_in", K)
        high_cut = sem("high_cut")
        low_cut = sem("low_cut")
        w1_cleared = sem("w1_cleared")
        dense_merged = sem("dense_merged")
        pad_set = sem("pad_set")
        ids_in = sems("ids_in", SLOTS)
        ids_wide_in = sem("ids_wide_in")
        dense_in = sems("dense_in", SLOTS * HALVES)
        rows_gathered = sems("rows_gathered", SLOTS * HALVES)
        rows_free = sems("rows_free", SLOTS * HALVES)
        gather_go = sem("gather_go")
        load_go = sem("load_go")
        onehot_made = sem("onehot_made")
        summed_up = sems("summed_up", 2)
        sums_out = sems("sums_out", 2)
        tiles_turned = sems("tiles_turned", 2)
        turned_out = sems("turned_out", 2)
        dots_summed = sems("dots_summed", 2)
        dots_out = sems("dots_out", 2)
        pairs_moved = sem("pairs_moved")
        y_stored = sems("y_stored", SLOTS)

        WEIGHT_LOADS = cols + 6

        block = ctx.enter_context(nc.Block())

        def stage_of(j):
            room = XT[:, :, :].rearrange("p b f -> p (b f)")
            return room[0:rows_p, chunk_at[j] * D:(chunk_at[j] + chunks[j]) * D]

        def part_of(part, j):
            return parts[part][:, chunk_at[j]:chunk_at[j] + chunks[j], :].rearrange("p c d -> p (c d)")

        ONEHOTS = [("onehot", j, j % 2) for j in range(K)]
        LAYERS = ([("layer1", m, m % 2) for m in range(m1)] + [("layer2", m, m % 2) for m in range(m2)]
                  + [("layer3", 0, 0)])

        def uses(items, q, upto=None):
            names = [item[:2] for item in items]
            end = names.index(upto) if upto else len(items)
            return sum(item[2] == q for item in items[:end])

        def use_number(step, what, i, q):
            if isinstance(step, int) and step == 0:
                return uses(ONEHOTS, q, (what, i))
            after = isinstance(step, int) and step == steps
            return (uses(ONEHOTS, q) + uses(ONEHOTS + LAYERS, q) * (step - 1)
                    + uses(LAYERS if after else ONEHOTS + LAYERS, q, (what, i)))

        def wait(eng, semaphore, value):
            if not (isinstance(value, int) and value == 0):
                eng.wait_ge(semaphore, value)

        def all_steps(eng, body):
            body(0, 0, 0)
            with eng.Fori(0, turns) as r:
                body(r * SLOTS + 1, r, 1)
                body(r * SLOTS + 2, r + 1, 0)
            body(steps - 1, turns, 1)

        @block.sync
        def _(sp):
            def load_step(step, s, r):
                sp.dma_start(ids[s][:, :, :],
                             ins["ids"][bass.ds(step * STEP, STEP), :].rearrange("(h p) f -> p h f", p=P)
                             ).then_inc(ids_in[s], 16)
                for h in range(HALVES):
                    k = HALVES * s + h
                    wait(sp, rows_free[k], r)
                    sp.sem_inc(load_go, 1)
                    sp.dma_start(rows_in[k][:, 0, :],
                                 ins["r_dense_features"][bass.ds(step * STEP + h * TILE, TILE), :]
                                 ).then_inc(dense_in[k], 16)

            def load_ids_wide(step):
                ids_of = ins["ids_summed"][:, bass.ds(step * STEP, STEP)]
                sp.dma_start(ids_wide[:, :, :], ids_of.rearrange("(o k) b -> o k b", o=1)
                             .broadcast_to([P, K, STEP])).then_inc(ids_wide_in, 16)

            load_step(0, 0, 0)
            load_ids_wide(0)
            for j in range(K):
                sp.dma_start(stage_of(j), tables[summed[j]].rearrange("(p c) d -> p (c d)", p=rows_p)
                             ).then_inc(tables_in[j], 16)
            load_step(1, 1, 0)
            sp.wait_ge(w1_cleared, 1)
            for f in range(cols):
                c, at, n = (f // 4, QUAD * (f % 4) + f + 1, cols - f) if f < native else fold_at[f - native]
                sp.dma_start(w1_pairs[at:at + n, c, :],
                             ins["W_top1"][D + base_of[f]:D + base_of[f] + n, :]).then_inc(weights_in, 16)
            sp.dma_start(w1_dense[:, :], ins["W_top1"][0:D, :]).then_inc(weights_in, 16)
            sp.dma_start(w1_dense_again[:, :], ins["W_top1"][D + n_pairs:, :]).then_inc(weights_in, 16)
            sp.dma_start(w2[:, :, :], ins["W_top2"].rearrange("(c p) n -> p c n", p=P)).then_inc(weights_in, 16)
            with nc.allow_non_contiguous_dma(reason="896 single numbers, once"):
                sp.dma_start(w3[:, :], ins["W_top3"].rearrange("(c p) o -> p (c o)", p=P)).then_inc(weights_in, 16)
                sp.dma_start(b1[:, :], ins["b_top1"].rearrange("(c p) -> p c", p=P)).then_inc(weights_in, 16)
                sp.dma_start(b2[:, :], ins["b_top2"].rearrange("(c p) -> p c", p=P)).then_inc(weights_in, 16)

            def body(step, r, s, ids_ahead=True, rows_ahead=True):
                if ids_ahead:
                    sp.wait_ge(onehot_made, K * (step + 1))
                    sp.sem_inc(load_go, 1)
                    load_ids_wide(step + 1)
                if rows_ahead:
                    for h in range(HALVES):
                        sp.wait_ge(rows_gathered[HALVES * s + h], 16 * NG * (r + 1))
                        sp.sem_inc(load_go, 1)
                    load_step(step + SLOTS, s, r + 1)
                if not (isinstance(step, int) and step == 0):
                    store_y(step - 1, 1 - s)
                for q in range(2):
                    sp.wait_ge(dots_out[q], HALVES * NGR // 2 * (step + 1))
                for i, (c, at, n) in enumerate(fold_at):
                    g = native + i + 1
                    sp.dma_start(z[at:at + n, c, :], short[g:g + n, i, :]).then_inc(pairs_moved, 16)

            def store_y(step, s):
                sp.wait_ge(sums_out[0], use_number(step + 1, "layer3", 0, 0) + 1)
                sp.sem_inc(load_go, 1)
                sp.dma_start(out[bass.ds(step * STEP, STEP), :].rearrange("b o -> o b"), y[s][:, :]
                             ).then_inc(y_stored[s], 16)

            body(0, 0, 0)
            with sp.Fori(0, turns - 1) as r:
                body(r * SLOTS + 1, r, 1)
                body(r * SLOTS + 2, r + 1, 0)
            body(steps - 3, turns - 1, 1)
            body(steps - 2, turns, 0, rows_ahead=False)
            body(steps - 1, turns, 1, ids_ahead=False, rows_ahead=False)
            store_y(steps - 1, 1)
            for s in range(SLOTS):
                sp.wait_ge(y_stored[s], 16 * (turns + 1))

        @block.gpsimd
        def _(pool):
            def gather(r, s, h):
                k = HALVES * s + h
                if not isinstance(r, int):
                    pool.wait_ge(rows_free[k], r)
                    pool.sem_inc(gather_go, 1)
                for i, t in enumerate(gathered):
                    pool.indirect_dma_start(
                        out=rows_in[k][:, 1 + i, :], out_offset=None, in_=tables[t],
                        in_offset=bass.IndirectOffsetOnAxis(ap=ids[s][:, h, t:t + 1], axis=0)
                    ).then_inc(rows_gathered[k], 16)

            nc.gpsimd.memset(ident[:, :], 0.0).then_inc(ident_made, 1)
            for n, col in row_number.items():
                nc.gpsimd.iota(col[:, :], [[1, n]], base=0, channel_multiplier=n,
                               allow_small_or_imprecise_dtypes=True).then_inc(rows_numbered, 1)
            pool.wait_ge(ident_made, 1)
            nc.gpsimd.affine_select(out=ident[:, :], in_=ident[:, :], compare_op=ALU.not_equal, fill=1.0,
                                    base=0, pattern=[[-1, P]], channel_multiplier=1).then_inc(ident_made, 1)
            def gather_turn(r):
                for s in range(SLOTS):
                    pool.wait_ge(ids_in[s], 16 * (r + 1))
                    pool.sem_inc(gather_go, 1)
                    for h in range(HALVES):
                        gather(r, s, h)

            gather_turn(0)
            with pool.Fori(1, turns + 1) as r:
                gather_turn(r)

        def copy_turned(eng, copy, q, step, s, h, i):
            if i < NB:
                b = batches[i]
                eng.wait_ge(tiles_turned[q], batches_of[q] * (step * HALVES + h) + i // 2 + 1)
                half = slice(h * TILE, (h + 1) * TILE)
                if i == 0:
                    copy(dense_T[s][:, half], turned[q][:, 0, :])
                f = b[0][1]
                copy(XT[:, half, f:f + len(b)],
                     turned[q][:, 0:len(b), :].rearrange("p f b -> p b f")).then_inc(turned_out[q], 1)

        def copy_dots(eng, copy, q, step, h):
            for i in range(q, NGR, 2):
                eng.wait_ge(dots_summed[q], NGR // 2 * (step * HALVES + h) + i // 2 + 1)
                for j in range(GROUP):
                    at = h * TILE + i * GPT * GROUP + j
                    samples = slice(at, at + (GPT - 1) * GROUP + 1, GROUP)
                    block_of = grams[q][QUAD * j:QUAD * j + feats, :, j * cols:(j + 1) * cols]
                    for quad in range(4):
                        copy(z[QUAD * quad:QUAD * quad + feats, :, samples],
                             block_of[:, :, quad:native:4].rearrange("p t f -> p f t"))
                    last = copy(short[:, :, samples], block_of[:, :, native:].rearrange("p t f -> p f t"))
                last.then_inc(dots_out[q], 1)

        @block.scalar
        def _(act):
            def copy(o, i):
                return nc.scalar.copy(o, i)

            for j in range(K):
                act.wait_ge(tables_in[j], 16)
                nc.scalar.copy(part_of(0, j), stage_of(j)).then_inc(high_cut, 1)
            act.wait_ge(weights_in, 16 * WEIGHT_LOADS)

            def copy_onehot(step, j):
                act.wait_ge(summed_up[j % 2], use_number(step, "onehot", j, j % 2) + 1)
                copy(XT[:, :, 1 + summed[j]], sums[j % 2][:, :]).then_inc(sums_out[j % 2], 1)

            def layer(step, what, h, b, n):
                for m in range(0, n, 2):
                    act.wait_ge(summed_up[0], use_number(step, what, m, 0) + 1)
                    nc.scalar.activation(h[:, m, :], sums[0][:, :], ACT.Relu,
                                         bias=b[:, m:m + 1]).then_inc(sums_out[0], 1)

            def layer3(step, r, s):
                act.wait_ge(summed_up[0], use_number(step, "layer3", 0, 0) + 1)
                wait(act, y_stored[s], 16 * r)
                copy(y[s][:, :], sums[0][0:1, :]).then_inc(sums_out[0], 1)

            def body(step, r, s):
                behind = not (isinstance(step, int) and step == 0)
                for k in range(3):
                    copy_turned(act, copy, 0, step, s, 0, 2 * k)
                    copy_onehot(step, k)
                for j in range(3, K):
                    copy_onehot(step, j)
                if behind:
                    layer(step, "layer1", h1, b1, m1)
                copy_dots(act, copy, 0, step, 0)
                copy_turned(act, copy, 0, step, s, 1, 0)
                if behind:
                    layer(step, "layer2", h2, b2, m2)
                copy_turned(act, copy, 0, step, s, 1, 2)
                copy_turned(act, copy, 0, step, s, 1, 4)
                if behind:
                    layer3(step, r - (1 - s), 1 - s)
                copy_dots(act, copy, 0, step, 1)

            all_steps(act, body)
            layer(steps, "layer1", h1, b1, m1)
            layer(steps, "layer2", h2, b2, m2)
            layer3(steps, turns, 1)

        @block.vector
        def _(dve):
            def copy(o, i):
                return nc.vector.tensor_copy(o, i)

            def make_onehot(step, j):
                if j % K == 0:
                    dve.wait_ge(ids_wide_in, 16 * (step + 1 + j // K))
                if j >= 2:
                    dve.wait_ge(summed_up[j % 2], use_number(step, "onehot", j - 2, j % 2) + 1)
                t = j % K
                col = row_number[chunks[t]]
                for c in range(chunks[t]):
                    last = nc.vector.tensor_scalar(onehot[j % 2][:, c, :], ids_wide[0:rows_p, t, :],
                                                   col[:, c:c + 1], None, ALU.is_equal)
                last.then_inc(onehot_made, 1)

            nc.vector.memset(z[:, :, :], 0.0).then_inc(pad_set, 1)
            nc.vector.memset(w1_pairs[:, :, :], 0.0).then_inc(w1_cleared, 1)
            dve.wait_ge(rows_numbered, len(row_number))
            for j in range(2):
                make_onehot(0, j)
            for j in range(K):
                dve.wait_ge(high_cut, j + 1)
                nc.vector.tensor_tensor(part_of(1, j), stage_of(j), part_of(0, j).bitcast(F32), ALU.subtract
                                        ).then_inc(low_cut, 1)
            dve.wait_ge(low_cut, K)
            nc.vector.memset(XT[:, :, feats:], 0.0).then_inc(pad_set, 1)

            def layer(step, what, h, b, n):
                for m in range(1, n, 2):
                    dve.wait_ge(summed_up[1], use_number(step, what, m, 1) + 1)
                    nc.vector.tensor_scalar(h[:, m, :], sums[1][:, :], b[:, m:m + 1], 0.0,
                                            ALU.add, ALU.max).then_inc(sums_out[1], 1)

            def body(step, r, s, ahead=True):
                behind = not (isinstance(step, int) and step == 0)
                for k in range(3):
                    copy_turned(dve, copy, 1, step, s, 0, 2 * k + 1)
                    if k:
                        make_onehot(step, k + 1)
                for j in range(4, K):
                    make_onehot(step, j)
                if behind:
                    layer(step, "layer1", h1, b1, m1)
                else:
                    dve.wait_ge(weights_in, 16 * WEIGHT_LOADS)
                    nc.vector.tensor_tensor(w1_dense[:, :], w1_dense[:, :], w1_dense_again, ALU.add
                                            ).then_inc(dense_merged, 1)
                copy_dots(dve, copy, 1, step, 0)
                copy_turned(dve, copy, 1, step, s, 1, 1)
                if behind:
                    layer(step, "layer2", h2, b2, m2)
                copy_turned(dve, copy, 1, step, s, 1, 3)
                copy_turned(dve, copy, 1, step, s, 1, 5)
                if ahead:
                    for j in range(K, K + 2):
                        make_onehot(step, j)
                copy_dots(dve, copy, 1, step, 1)

            body(0, 0, 0)
            with dve.Fori(0, turns) as r:
                body(r * SLOTS + 1, r, 1)
                body(r * SLOTS + 2, r + 1, 0)
            body(steps - 1, turns, 1, ahead=False)
            layer(steps, "layer1", h1, b1, m1)
            layer(steps, "layer2", h2, b2, m2)

        @block.tensor
        def _(pe):
            def onehot_sums(step, j):
                q = j % 2
                if isinstance(step, int) and step == 0:
                    pe.wait_ge(low_cut, j + 1)
                pe.wait_ge(onehot_made, K * step + j + 1)
                wait(pe, sums_out[q], use_number(step, "onehot", j, q))
                for c in range(chunks[j]):
                    for part in range(PARTS):
                        last = nc.tensor.matmul(sums[q][:, :], parts[part][:, chunk_at[j] + c, :],
                                                onehot[q][:, c, :], start=(c == 0 and part == 0),
                                                stop=(c == chunks[j] - 1 and part == PARTS - 1))
                last.then_inc(summed_up[q], 1)

            def transposes(step, r, s, h, i):
                k = HALVES * s + h
                if i == 0:
                    pe.wait_ge(dense_in[k], 16 * (r + 1))
                    pe.wait_ge(rows_gathered[k], 16 * NG * (r + 1))
                if i < NB:
                    q = i % 2
                    wait(pe, turned_out[q], batches_of[q] * (step * HALVES + h) + i // 2)
                    for n, (place, _) in enumerate(batches[i]):
                        last = nc.tensor.transpose(turned[q][:, n, :], rows_in[k][:, place, :], ident[:, :])
                    last.then_inc(tiles_turned[q], 1)

            def dot_products(step, s, h):
                for q in range(2):
                    pe.wait_ge(turned_out[q], batches_of[q] * (step * HALVES + h + 1))
                    if h == 0:
                        last_table = max(j for j in range(K) if j % 2 == q)
                        pe.wait_ge(sums_out[q], use_number(step, "onehot", last_table, q) + 1)
                for i in range(NGR):
                    q = i % 2
                    wait(pe, dots_out[q], NGR // 2 * (step * HALVES + h) + i // 2)
                    for t in range(GPT):
                        b0 = h * TILE + (i * GPT + t) * GROUP
                        four = XT[:, b0:b0 + GROUP, :]
                        last = nc.tensor.matmul(grams[q][:, t, 0:GROUP * cols].rearrange("p (b f) -> p b f", f=cols),
                                                four.rearrange("p b f -> p (b f)"), four[:, :, 0:cols], start=True, stop=True)
                        if i == t == 0:
                            last.then_inc(rows_free[HALVES * s + h], 1)
                    last.then_inc(dots_summed[q], 1)

            def layer1(step, s):
                pe.wait_ge(pairs_moved, PAIRS_DONE * step)
                for m in range(m1):
                    q = m % 2
                    pe.wait_ge(sums_out[q], use_number(step, "layer1", m, q))
                    nc.tensor.matmul(sums[q][:, :], w1_dense[:, m * P:(m + 1) * P], dense_T[s][:, :],
                                     start=True, stop=False)
                    for c in range(ZC):
                        last = nc.tensor.matmul(sums[q][:, :], w1_pairs[:, c, m * P:(m + 1) * P],
                                                z[:, c, :], start=False, stop=(c == ZC - 1))
                    last.then_inc(summed_up[q], 1)

            def layer2(step, m):
                if m == 0:
                    for q in range(2):
                        pe.wait_ge(sums_out[q], use_number(step, "layer1", m1 - 2 + q, q) + 1)
                q = m % 2
                pe.wait_ge(sums_out[q], use_number(step, "layer2", m, q))
                for c in range(m1):
                    last = nc.tensor.matmul(sums[q][:, :], w2[:, c, m * P:(m + 1) * P], h1[:, c, :],
                                            start=(c == 0), stop=(c == m1 - 1))
                last.then_inc(summed_up[q], 1)

            def layer3(step):
                for q in range(2):
                    pe.wait_ge(sums_out[q], use_number(step, "layer2", m2 - 2 + q, q) + 1)
                pe.wait_ge(sums_out[0], use_number(step, "layer3", 0, 0))
                for c in range(m2):
                    last = nc.tensor.matmul(sums[0][0:1, :], w3[:, c:c + 1], h2[:, c, :],
                                            start=(c == 0), stop=(c == m2 - 1))
                last.then_inc(summed_up[0], 1)

            pe.wait_ge(ident_made, 2)
            pe.wait_ge(pad_set, 2)

            def body(step, r, s):
                behind = not (isinstance(step, int) and step == 0)
                for k in range(3):
                    transposes(step, r, s, 0, 2 * k)
                    transposes(step, r, s, 0, 2 * k + 1)
                    onehot_sums(step, k)
                for j in range(3, K):
                    onehot_sums(step, j)
                if behind:
                    layer1(step, 1 - s)
                dot_products(step, s, 0)
                for k in range(3):
                    transposes(step, r, s, 1, 2 * k)
                    transposes(step, r, s, 1, 2 * k + 1)
                    if behind and k < m2:
                        layer2(step, k)
                if behind:
                    layer3(step)
                else:
                    pe.wait_ge(weights_in, 16 * WEIGHT_LOADS)
                    pe.wait_ge(dense_merged, 1)
                dot_products(step, s, 1)

            all_steps(pe, body)
            layer1(steps, 1)
            layer2(steps, 0)
            layer2(steps, 1)
            layer3(steps)


def kernel(**inputs):
    import concourse.bacc as bacc
    from concourse.bass_utils import run_bass_kernel_spmd

    nc = bacc.Bacc("TRN2", target_bir_lowering=False, num_devices=1)
    given = dict(inputs, ids_summed=np.asarray(inputs["ids"]).T[list(SUMMED)])
    arrays, ins = {}, {}
    for name, value in given.items():
        a = np.ascontiguousarray(value)
        arrays[f"in_{name}"] = a
        ins[name] = nc.dram_tensor(f"in_{name}", a.shape, mybir.dt.from_np(a.dtype), kind="ExternalInput").ap()
    n = arrays["in_ids"].shape[0]
    out = nc.dram_tensor("out_y", (n, 1), F32, kind="ExternalOutput").ap()
    dlrm_kernel(nc, ins, out)
    return run_bass_kernel_spmd(nc, [arrays], core_ids=[0]).results[0]["out_y"]
```

```python
from contextlib import ExitStack

import numpy as np

import concourse.bass as bass
from concourse import mybir

F32 = mybir.dt.float32
F32R = mybir.dt.float32r
I32 = mybir.dt.int32
ALU = mybir.AluOpType
ACT = mybir.ActivationFunctionType

SUMMED = (24, 2, 10, 15, 16, 21, 25)
P = 128
D = 128
QUAD = 32
GROUP = 4
TILE = 128
HALVES = 2
STEP = TILE * HALVES
SLOTS = 2
AHEAD = 3
PARTS = 2
GPSIMD_MOVES = 3


def dlrm_kernel(nc, ins, out):
    n_samples, n_tables = ins["ids"].shape
    feats = n_tables + 1
    cols = feats - 1
    n_pairs = feats * cols // 2
    steps = n_samples // STEP
    turns = (steps - 2) // SLOTS
    tables = [ins[f"tbl_{t}"] for t in range(n_tables)]
    hid1, hid2 = ins["W_top2"].shape
    m1, m2 = hid1 // P, hid2 // P

    summed = list(SUMMED)
    K = len(summed)
    rows_p = 125
    chunks = [tables[t].shape[0] // rows_p for t in summed]
    assert all(tables[t].shape[0] == rows_p * c for t, c in zip(summed, chunks))
    chunk_at = [sum(chunks[:j]) for j in range(K)]
    gathered = [t for t in range(n_tables) if t not in summed]
    NG = len(gathered)
    rows = [(0, 0)] + [(1 + i, 1 + t) for i, t in enumerate(gathered)]
    batches = []
    for place, feat in rows:
        if batches and len(batches[-1]) < 4 and batches[-1][-1][1] == feat - 1:
            batches[-1].append((place, feat))
        else:
            batches.append([(place, feat)])
    NB = len(batches)
    gathers_of = [sum(place > 0 for place, _ in b) for b in batches]
    batches_of = [(NB + 1) // 2, NB // 2]
    GPT = 8
    NGR = TILE // GROUP // GPT

    base_of = [sum(cols - e for e in range(f)) for f in range(cols)]
    ZC = 4
    native = ZC * (P // QUAD)
    folded = cols - native
    fold_at = [((native - 1 - i) // 4, QUAD * ((native - 1 - i) % 4), folded - i) for i in range(folded)]
    assert all(n <= native - i for i, (_, _, n) in enumerate(fold_at))
    PAIRS_DONE = 16 * folded
    WHOLE = [ZC, *range(ZC)]
    LAST_PIECES = [WHOLE[0:3], WHOLE[3:]]

    with ExitStack() as ctx:
        def sb(name, shape, dt=F32):
            return ctx.enter_context(nc.sbuf_tensor(name, shape, dt))

        def ps(name, shape):
            return ctx.enter_context(nc.psum_tensor(name, shape, F32))

        def sem(name):
            return ctx.enter_context(nc.semaphore(name))

        def sems(name, n):
            return [sem(f"{name}{i}") for i in range(n)]

        ident = sb("ident", [P, P])
        row_number = {c: sb(f"row_number{c}", [rows_p, c]) for c in sorted(set(chunks))}
        w1_parts = [sb(f"w1_part{q}", [P, ZC + 1, hid1], F32R) for q in range(PARTS)]
        w2_parts = [sb(f"w2_part{q}", [P, m1, hid2], F32R) for q in range(PARTS)]
        w_parts = [w1_parts, w2_parts]
        w3 = sb("w3", [P, m2])
        b1 = sb("b1", [P, m1])
        b2 = sb("b2", [P, m2])
        parts = [sb(f"parts{q}", [rows_p, sum(chunks), D], F32R) for q in range(PARTS)]
        ids = [sb(f"ids{s}", [P, HALVES, n_tables], I32) for s in range(SLOTS)]
        ids_wide = sb("ids_wide", [P, K - 1, STEP], I32)
        rows_in = [sb(f"rows_in{s}", [P, 1 + NG, D]) for s in range(HALVES)]
        onehot = [sb(f"onehot{q}", [rows_p, max(chunks[q::AHEAD]), STEP], F32R) for q in range(AHEAD)]
        XT = sb("XT", [P, STEP, QUAD])
        dense_T = [sb(f"dense_T{s}", [P, STEP]) for s in range(SLOTS)]
        z = sb("z", [P, ZC, STEP])
        z_parts = [sb(f"z_part{q}", [P, ZC + 1, STEP], F32R) for q in range(PARTS)]
        h1_parts = [sb(f"h1_part{q}", [P, m1, STEP], F32R) for q in range(PARTS)]
        short = sb("short", [P, folded, STEP])
        h1 = sb("h1", [P, 2, STEP])
        w1_dense_again = h1[:, :, :].rearrange("p m b -> p (m b)")[:, 0:hid1]
        assert folded * STEP == (ZC + 1) * hid1 and ZC * STEP == m1 * hid2
        w_stage = [short[:, :, :].rearrange("p f b -> p (f b)").rearrange("p (c n) -> p c n", n=hid1),
                   z[:, :, :].rearrange("p c b -> p (c b)").rearrange("p (c n) -> p c n", n=hid2)]
        assert m2 == 2
        h2 = h1
        y = [short[QUAD:QUAD + 1, s, :] for s in range(SLOTS)]

        turned = [ps(f"turned{q}", [P, 4, TILE]) for q in range(2)]
        grams = [ps(f"grams{q}", [P, GPT, P]) for q in range(2)]
        sums = [ps(f"sums{q}", [P, STEP]) for q in range(2)]

        ident_made = sem("ident_made")
        rows_numbered = sem("rows_numbered")
        weights_in = sem("weights_in")
        tables_in = sems("tables_in", K)
        high_cut = sem("high_cut")
        low_cut = sem("low_cut")
        w1_cleared = sem("w1_cleared")
        dense_merged = sem("dense_merged")
        weights_high = sem("weights_high")
        weights_cut = sem("weights_cut")
        pad_set = sem("pad_set")
        z_high = sem("z_high")
        z_cut = sem("z_cut")
        h1_cut = sem("h1_cut")
        ids_in = sems("ids_in", SLOTS)
        ids_wide_in = sems("ids_wide_in", 2)
        dense_in = sems("dense_in", HALVES)
        rows_gathered = [sems(f"rows_gathered{k}_", NB) for k in range(HALVES)]
        rows_free = sems("rows_free", HALVES)
        gather_go = sem("gather_go")
        load_go = sem("load_go")
        onehot_made = sem("onehot_made")
        summed_up = sems("summed_up", 2)
        sums_out = sems("sums_out", 2)
        tiles_turned = sems("tiles_turned", 2)
        turned_out = sems("turned_out", 2)
        dots_summed = sems("dots_summed", 2)
        dots_out = sems("dots_out", 2)
        pairs_moved = sem("pairs_moved")
        last_pairs_moved = sem("last_pairs_moved")
        y_stored = sems("y_stored", SLOTS)

        WEIGHT_LOADS = cols + 6

        block = ctx.enter_context(nc.Block())

        def stage_of(j):
            room = XT[:, :, :].rearrange("p b f -> p (b f)")
            return room[0:rows_p, chunk_at[j] * D:(chunk_at[j] + chunks[j]) * D]

        def part_of(part, j):
            return parts[part][:, chunk_at[j]:chunk_at[j] + chunks[j], :].rearrange("p c d -> p (c d)")

        ONEHOTS = [("onehot", j, j % 2) for j in range(K)]
        blocks = [("layer1", m) for m in range(m1)] + [("layer2", m) for m in range(m2)] + [("layer3", 0)]
        LAYERS = [(what, m, (K + i) % 2) for i, (what, m) in enumerate(blocks)]
        bank_of = {(what, m): q for what, m, q in LAYERS}

        def uses(items, q, upto=None):
            names = [item[:2] for item in items]
            end = names.index(upto) if upto else len(items)
            return sum(item[2] == q for item in items[:end])

        def use_number(step, what, i, q):
            if isinstance(step, int) and step == 0:
                return uses(ONEHOTS, q, (what, i))
            after = isinstance(step, int) and step == steps
            return (uses(ONEHOTS, q) + uses(ONEHOTS + LAYERS, q) * (step - 1)
                    + uses(LAYERS if after else ONEHOTS + LAYERS, q, (what, i)))

        def wait(eng, semaphore, value):
            if not (isinstance(value, int) and value == 0):
                eng.wait_ge(semaphore, value)

        def wait_past(eng, semaphore, value):
            wait(eng, semaphore, max(value, 0) if isinstance(value, int) else value)

        def move_pairs(eng, step, of, moved):
            for q in range(2):
                eng.wait_ge(dots_out[q], HALVES * NGR * (step + 1))
            for i in of:
                c, at, n = fold_at[i]
                g = native + i + 1
                eng.dma_start(z[at:at + n, c, :], short[g:g + n, i, :]).then_inc(moved, 16)

        def all_steps(eng, body):
            body(0, 0, 0)
            with eng.Fori(0, turns) as r:
                body(r * SLOTS + 1, r, 1)
                body(r * SLOTS + 2, r + 1, 0)
            body(steps - 1, turns, 1, last_step=True)

        @block.sync
        def _(sp):
            def load_ids(step, s):
                sp.dma_start(ids[s][:, :, :],
                             ins["ids"][bass.ds(step * STEP, STEP), :].rearrange("(h p) f -> p h f", p=P)
                             ).then_inc(ids_in[s], 16)

            def load_dense(step, h):
                if not (isinstance(step, int) and step == 0):
                    sp.wait_ge(rows_free[h], step)
                    sp.sem_inc(load_go, 1)
                sp.dma_start(rows_in[h][:, 0, :],
                             ins["r_dense_features"][bass.ds(step * STEP + h * TILE, TILE), :]
                             ).then_inc(dense_in[h], 16)

            def load_ids_wide(step, last):
                of, n = (slice(K - 1, K), 1) if last else (slice(0, K - 1), K - 1)
                sp.dma_start(ids_wide[:, 0:n, :],
                             ins["ids_summed"][of, bass.ds(step * STEP, STEP)].rearrange("(o k) b -> o k b", o=1)
                             .broadcast_to([P, n, STEP])).then_inc(ids_wide_in[last], 16)

            load_ids(0, 0)
            load_ids_wide(0, 0)
            for j in range(K):
                sp.dma_start(stage_of(j), tables[summed[j]].rearrange("(p c) d -> p (c d)", p=rows_p)
                             ).then_inc(tables_in[j], 16)
            for h in range(HALVES):
                load_dense(0, h)
            load_ids(1, 1)
            sp.wait_ge(onehot_made, 1)
            load_ids_wide(0, 1)
            sp.wait_ge(w1_cleared, 1)
            for f in range(cols):
                c, at, n = (f // 4, QUAD * (f % 4) + f + 1, cols - f) if f < native else fold_at[f - native]
                sp.dma_start(w_stage[0][at:at + n, c, :],
                             ins["W_top1"][D + base_of[f]:D + base_of[f] + n, :]).then_inc(weights_in, 16)
            sp.dma_start(w_stage[0][:, ZC, :], ins["W_top1"][0:D, :]).then_inc(weights_in, 16)
            sp.dma_start(w1_dense_again, ins["W_top1"][D + n_pairs:, :]).then_inc(weights_in, 16)
            sp.dma_start(w_stage[1], ins["W_top2"].rearrange("(c p) n -> p c n", p=P)).then_inc(weights_in, 16)
            with nc.allow_non_contiguous_dma(reason="896 single numbers, once"):
                sp.dma_start(w3[:, :], ins["W_top3"].rearrange("(c p) o -> p (c o)", p=P)).then_inc(weights_in, 16)
                sp.dma_start(b1[:, :], ins["b_top1"].rearrange("(c p) -> p c", p=P)).then_inc(weights_in, 16)
                sp.dma_start(b2[:, :], ins["b_top2"].rearrange("(c p) -> p c", p=P)).then_inc(weights_in, 16)

            def body(step, s, rows_ahead=True, ids_ahead=True, last_step=False):
                if rows_ahead:
                    sp.wait_ge(onehot_made, K * (step + 1))
                    sp.sem_inc(load_go, 1)
                    load_ids_wide(step + 1, 0)
                    load_dense(step + 1, 0)
                    sp.wait_ge(onehot_made, K * (step + 1) + 1)
                    sp.sem_inc(load_go, 1)
                    load_ids_wide(step + 1, 1)
                    load_dense(step + 1, 1)
                if ids_ahead:
                    load_ids(step + SLOTS, s)
                if not (isinstance(step, int) and step == 0 or last_step):
                    store_y(step - 1, 1 - s)
                move_pairs(sp, step, range(GPSIMD_MOVES if last_step else 0, folded), pairs_moved)
                if last_step:
                    store_y(step - 1, 1 - s)

            def store_y(step, s):
                q = bank_of["layer3", 0]
                sp.wait_ge(sums_out[q], use_number(step + 1, "layer3", 0, q) + 1)
                sp.sem_inc(load_go, 1)
                sp.dma_start(out[bass.ds(step * STEP, STEP), :].rearrange("b o -> o b"), y[s]
                             ).then_inc(y_stored[s], 16)

            body(0, 0)
            with sp.Fori(0, turns - 1) as r:
                body(r * SLOTS + 1, 1)
                body(r * SLOTS + 2, 0)
            body(steps - 3, 1)
            body(steps - 2, 0, ids_ahead=False)
            body(steps - 1, 1, rows_ahead=False, ids_ahead=False, last_step=True)
            store_y(steps - 1, 1)
            for s in range(SLOTS):
                sp.wait_ge(y_stored[s], 16 * (turns + 1))

        @block.gpsimd
        def _(pool):
            def gather(step, s, h):
                if not (isinstance(step, int) and step == 0):
                    pool.wait_ge(rows_free[h], step)
                    pool.sem_inc(gather_go, 1)
                for i, b in enumerate(batches):
                    for place, feat in b:
                        if place:
                            t = feat - 1
                            pool.indirect_dma_start(
                                out=rows_in[h][:, place, :], out_offset=None, in_=tables[t],
                                in_offset=bass.IndirectOffsetOnAxis(ap=ids[s][:, h, t:t + 1], axis=0)
                            ).then_inc(rows_gathered[h][i], 16)

            nc.gpsimd.memset(ident[:, :], 0.0).then_inc(ident_made, 1)
            for n, col in row_number.items():
                nc.gpsimd.iota(col[:, :], [[1, n]], base=0, channel_multiplier=n,
                               allow_small_or_imprecise_dtypes=True).then_inc(rows_numbered, 1)
            pool.wait_ge(ident_made, 1)
            nc.gpsimd.affine_select(out=ident[:, :], in_=ident[:, :], compare_op=ALU.not_equal, fill=1.0,
                                    base=0, pattern=[[-1, P]], channel_multiplier=1).then_inc(ident_made, 1)

            def gather_turn(r):
                for s in range(SLOTS):
                    pool.wait_ge(ids_in[s], 16 * (r + 1))
                    pool.sem_inc(gather_go, 1)
                    for h in range(HALVES):
                        gather(r * SLOTS + s, s, h)

            gather_turn(0)
            with pool.Fori(1, turns + 1) as r:
                gather_turn(r)
            move_pairs(pool, steps - 1, range(GPSIMD_MOVES), last_pairs_moved)

        def copy_turned(eng, copy, q, step, s, h, i):
            if i < NB:
                b = batches[i]
                eng.wait_ge(tiles_turned[q], batches_of[q] * (step * HALVES + h) + i // 2 + 1)
                half = slice(h * TILE, (h + 1) * TILE)
                if i == 0:
                    copy(dense_T[s][:, half], turned[q][:, 0, :])
                f = b[0][1]
                copy(XT[:, half, f:f + len(b)],
                     turned[q][:, 0:len(b), :].rearrange("p f b -> p b f")).then_inc(turned_out[q], 1)

        def copy_dots(eng, copy, q, step, h, tiles=range(NGR)):
            for i in tiles:
                eng.wait_ge(dots_summed[i % 2], NGR // 2 * (step * HALVES + h) + i // 2 + 1)
                for j in (2 * q, 2 * q + 1):
                    at = h * TILE + i * GPT * GROUP + j
                    samples = slice(at, at + (GPT - 1) * GROUP + 1, GROUP)
                    block_of = grams[i % 2][QUAD * j:QUAD * j + feats, :, j * cols:(j + 1) * cols]
                    for quad in range(4):
                        copy(z[QUAD * quad:QUAD * quad + feats, :, samples],
                             block_of[:, :, quad:native:4].rearrange("p t f -> p f t"))
                    last = copy(short[0:feats, :, samples], block_of[:, :, native:].rearrange("p t f -> p f t"))
                last.then_inc(dots_out[q], 1)

        @block.scalar
        def _(act):
            def copy(o, i):
                return nc.scalar.copy(o, i)

            for j in range(K):
                act.wait_ge(tables_in[j], 16)
                nc.scalar.copy(part_of(0, j), stage_of(j)).then_inc(high_cut, 1)

            def copy_onehot(step, j):
                act.wait_ge(summed_up[j % 2], use_number(step, "onehot", j, j % 2) + 1)
                copy(XT[:, :, 1 + summed[j]], sums[j % 2][:, :]).then_inc(sums_out[j % 2], 1)

            def cut_weights_high():
                act.wait_ge(weights_in, 16 * WEIGHT_LOADS)
                act.wait_ge(dense_merged, 1)
                for stage, (high, _) in zip(w_stage, w_parts):
                    nc.scalar.copy(high[:, :, :], stage).then_inc(weights_high, 1)

            def cut_z_high(step, s, piece=WHOLE):
                if isinstance(step, int) and step == steps:
                    act.wait_ge(pairs_moved, PAIRS_DONE * step - 16 * GPSIMD_MOVES)
                    act.wait_ge(last_pairs_moved, 16 * GPSIMD_MOVES)
                else:
                    act.wait_ge(pairs_moved, PAIRS_DONE * step)
                if ZC in piece:
                    last = nc.scalar.copy(z_parts[0][:, ZC, :], dense_T[s][:, :])
                here = slice(min(piece), [c for c in piece if c < ZC][-1] + 1)
                last = nc.scalar.copy(z_parts[0][:, here, :], z[:, here, :])
                last.then_inc(z_high, 1)

            def layer(step, what, to, b, ms):
                for m in ms:
                    q = bank_of[what, m]
                    act.wait_ge(summed_up[q], use_number(step, what, m, q) + 1)
                    if what == "layer1" and m >= 2:
                        act.wait_ge(h1_cut, m1 * (step - 1) + m - 1)
                    for h in to:
                        last = nc.scalar.activation(h[:, m if h is h1_parts[0] else m % 2, :], sums[q][:, :], ACT.Relu, bias=b[:, m:m + 1])
                    last.then_inc(sums_out[q], 1)

            def layer3(step, r, s):
                q = bank_of["layer3", 0]
                act.wait_ge(summed_up[q], use_number(step, "layer3", 0, q) + 1)
                wait(act, y_stored[s], 16 * r)
                copy(y[s], sums[q][0:1, :]).then_inc(sums_out[q], 1)

            def body(step, r, s, last_step=False):
                behind = not (isinstance(step, int) and step == 0)
                if not behind:
                    act.wait_ge(low_cut, K)
                    for j in range(K - 2):
                        copy_onehot(step, j)
                    cut_weights_high()
                    for j in range(K - 2, K):
                        copy_onehot(step, j)
                else:
                    for j in range(K - 3):
                        copy_onehot(step, j)
                for k in range(3):
                    copy_turned(act, copy, 0, step, s, 0, 2 * k)
                    if behind and k == 1:
                        cut_z_high(step, 1 - s)
                    if behind:
                        copy_onehot(step, K - 3 + k)
                if behind:
                    layer(step, "layer1", (h1_parts[0], h1), b1, [0])
                    act.wait_ge(z_cut, step)
                else:
                    act.wait_ge(pad_set, 2)
                copy_dots(act, copy, 0, step, 0)
                if last_step:
                    for k in range(3):
                        copy_turned(act, copy, 0, step, s, 1, 2 * k)
                    copy_dots(act, copy, 0, step, 1)
                if behind:
                    layer(step, "layer1", (h1_parts[0], h1), b1, range(1, m1))
                for k in range(3):
                    if last_step and k < len(LAST_PIECES):
                        cut_z_high(steps, s, LAST_PIECES[k])
                    if not last_step:
                        copy_turned(act, copy, 0, step, s, 1, 2 * k)
                    if behind and k < m2:
                        layer(step, "layer2", (h2,), b2, [k])
                if behind:
                    layer3(step, r - (1 - s), 1 - s)
                if not last_step:
                    copy_dots(act, copy, 0, step, 1)

            all_steps(act, body)
            layer(steps, "layer1", (h1_parts[0], h1), b1, range(m1))
            layer(steps, "layer2", (h2,), b2, range(m2))
            layer3(steps, turns, 1)

        @block.vector
        def _(dve):
            def copy(o, i):
                return nc.vector.tensor_copy(o, i)

            def make_onehot(step, j):
                t = j % K
                if t in (0, K - 1):
                    dve.wait_ge(ids_wide_in[t == K - 1], 16 * (step + 1 + j // K))
                if j >= AHEAD:
                    former = t - AHEAD if t >= AHEAD else max(range(t, K, AHEAD))
                    dve.wait_ge(summed_up[former % 2], use_number(step, "onehot", former, former % 2) + 1)
                col = row_number[chunks[t]]
                for c in range(chunks[t]):
                    last = nc.vector.tensor_scalar(onehot[t % AHEAD][:, c, :], ids_wide[0:rows_p, t % (K - 1), :],
                                                   col[:, c:c + 1], None, ALU.is_equal)
                last.then_inc(onehot_made, 1)

            nc.vector.memset(w_stage[0][:, 0:ZC, :], 0.0).then_inc(w1_cleared, 1)
            dve.wait_ge(rows_numbered, len(row_number))
            for j in range(AHEAD):
                make_onehot(0, j)
            for j in range(K):
                dve.wait_ge(high_cut, j + 1)
                nc.vector.tensor_tensor(part_of(1, j), stage_of(j), part_of(0, j).bitcast(F32), ALU.subtract
                                        ).then_inc(low_cut, 1)
            dve.wait_ge(low_cut, K)
            nc.vector.memset(XT[:, :, feats:], 0.0).then_inc(pad_set, 1)

            def cut_z_low(step, s, piece=WHOLE, pieces_before=0):
                dve.wait_ge(z_high, step + pieces_before)
                if ZC in piece:
                    nc.vector.tensor_tensor(z_parts[1][:, ZC, :], dense_T[s][:, :],
                                            z_parts[0][:, ZC, :].bitcast(F32), ALU.subtract)
                here = slice(min(piece), [c for c in piece if c < ZC][-1] + 1)
                nc.vector.tensor_tensor(z_parts[1][:, here, :], z[:, here, :],
                                        z_parts[0][:, here, :].bitcast(F32), ALU.subtract).then_inc(z_cut, 1)

            def cut_h1_low(step, m):
                q = bank_of["layer1", m]
                dve.wait_ge(sums_out[q], use_number(step, "layer1", m, q) + 1)
                nc.vector.tensor_tensor(h1_parts[1][:, m, :], h1[:, m % 2, :],
                                        h1_parts[0][:, m, :].bitcast(F32), ALU.subtract
                                        ).then_inc(h1_cut, 1)

            def merge_dense():
                dve.wait_ge(weights_in, 16 * WEIGHT_LOADS)
                nc.vector.tensor_tensor(w_stage[0][:, ZC, :], w_stage[0][:, ZC, :], w1_dense_again, ALU.add
                                        ).then_inc(dense_merged, 1)

            def cut_weights_low(i):
                dve.wait_ge(weights_high, i + 1)
                high, low = w_parts[i]
                nc.vector.tensor_tensor(low[:, :, :], w_stage[i], high[:, :, :].bitcast(F32), ALU.subtract
                                        ).then_inc(weights_cut, 1)

            def body(step, r, s, last_step=False):
                behind = not (isinstance(step, int) and step == 0)
                for j in range(AHEAD, K - 1):
                    make_onehot(step, j)
                if not behind:
                    merge_dense()
                    make_onehot(step, K - 1)
                    cut_weights_low(0)
                copy_turned(dve, copy, 1, step, s, 0, 1)
                if behind:
                    make_onehot(step, K - 1)
                    copy_turned(dve, copy, 1, step, s, 0, 3)
                    cut_z_low(step, 1 - s)
                    copy_turned(dve, copy, 1, step, s, 0, 5)
                    cut_h1_low(step, 0)
                    dve.wait_ge(z_cut, step)
                else:
                    cut_weights_low(1)
                    copy_turned(dve, copy, 1, step, s, 0, 3)
                    dve.wait_ge(weights_cut, 2)
                    nc.vector.memset(z[:, :, :], 0.0).then_inc(pad_set, 1)
                    copy_turned(dve, copy, 1, step, s, 0, 5)
                    dve.wait_ge(pad_set, 2)
                copy_dots(dve, copy, 1, step, 0)
                if last_step:
                    for i in (1, 3, 5):
                        copy_turned(dve, copy, 1, step, s, 1, i)
                    copy_dots(dve, copy, 1, step, 1)
                    for m in range(1, m1):
                        cut_h1_low(step, m)
                    for i, piece in enumerate(LAST_PIECES):
                        cut_z_low(steps, s, piece, i)
                    return
                if behind:
                    make_onehot(step, K)
                    for m in range(1, m1):
                        cut_h1_low(step, m)
                copy_turned(dve, copy, 1, step, s, 1, 1)
                if behind:
                    make_onehot(step, K + 1)
                copy_turned(dve, copy, 1, step, s, 1, 3)
                copy_turned(dve, copy, 1, step, s, 1, 5)
                make_onehot(step, K + 2 if behind else K)
                copy_dots(dve, copy, 1, step, 1, range(2))
                if not behind:
                    make_onehot(step, K + 1)
                copy_dots(dve, copy, 1, step, 1, range(2, NGR))
                if not behind:
                    make_onehot(step, K + 2)

            all_steps(dve, body)
            for m in range(m1):
                cut_h1_low(steps, m)

        @block.tensor
        def _(pe):
            def onehot_sums(step, j, frees=False):
                q = j % 2
                if isinstance(step, int) and step == 0:
                    pe.wait_ge(low_cut, j + 1)
                pe.wait_ge(onehot_made, K * step + j + 1)
                wait(pe, sums_out[q], use_number(step, "onehot", j, q))
                for c in range(chunks[j]):
                    for part in range(PARTS):
                        if frees and (c, part) == (0, 1):
                            last.then_inc(rows_free[0], 1)
                        last = nc.tensor.matmul(sums[q][:, :], parts[part][:, chunk_at[j] + c, :],
                                                onehot[j % AHEAD][:, c, :], start=(c == 0 and part == 0),
                                                stop=(c == chunks[j] - 1 and part == PARTS - 1))
                last.then_inc(summed_up[q], 1)

            def transposes(step, h, i):
                if i == 0:
                    pe.wait_ge(dense_in[h], 16 * (step + 1))
                if i < NB:
                    pe.wait_ge(rows_gathered[h][i], 16 * gathers_of[i] * (step + 1))
                if i < NB:
                    q = i % 2
                    wait(pe, turned_out[q], batches_of[q] * (step * HALVES + h) + i // 2)
                    for n, (place, _) in enumerate(batches[i]):
                        last = nc.tensor.transpose(turned[q][:, n, :], rows_in[h][:, place, :], ident[:, :])
                    last.then_inc(tiles_turned[q], 1)

            def dot_products(step, h, frees=True):
                for q in range(2):
                    pe.wait_ge(turned_out[q], batches_of[q] * (step * HALVES + h + 1))
                    if h == 0:
                        last_table = max(j for j in range(K) if j % 2 == q)
                        pe.wait_ge(sums_out[q], use_number(step, "onehot", last_table, q) + 1)
                for i in range(NGR):
                    q = i % 2
                    for reader in range(2):
                        wait_past(pe, dots_out[reader], NGR * (step * HALVES + h) + i - 1)
                    for t in range(GPT):
                        b0 = h * TILE + (i * GPT + t) * GROUP
                        four = XT[:, b0:b0 + GROUP, :]
                        last = nc.tensor.matmul(grams[q][:, t, 0:GROUP * cols].rearrange("p (b f) -> p b f", f=cols),
                                                four.rearrange("p b f -> p (b f)"), four[:, :, 0:cols], start=True, stop=True)
                        if i == t == 0 and frees:
                            last.then_inc(rows_free[h], 1)
                    last.then_inc(dots_summed[q], 1)

            PASSES = ((0, 0), (1, 0), (0, 1))

            def layer1(step, ms=range(m1)):
                after = isinstance(step, int) and step == steps
                if not after:
                    pe.wait_ge(z_cut, step)
                for m in ms:
                    q = bank_of["layer1", m]
                    pe.wait_ge(sums_out[q], use_number(step, "layer1", m, q))
                    for c in WHOLE:
                        for k, piece in enumerate(LAST_PIECES):
                            if after and m == 0 and c == piece[0]:
                                pe.wait_ge(z_cut, step + k)
                        for i, (w, x) in enumerate(PASSES):
                            last = nc.tensor.matmul(sums[q][:, :], w1_parts[w][:, c, m * P:(m + 1) * P],
                                                    z_parts[x][:, c, :], start=(c == WHOLE[0] and i == 0),
                                                    stop=(c == WHOLE[-1] and i == len(PASSES) - 1))
                    last.then_inc(summed_up[q], 1)

            def layer2(step, m):
                q = bank_of["layer2", m]
                pe.wait_ge(sums_out[q], use_number(step, "layer2", m, q))
                for c in range(m1):
                    if m == 0:
                        pe.wait_ge(h1_cut, m1 * (step - 1) + c + 1)
                    for i, (w, x) in enumerate(PASSES):
                        last = nc.tensor.matmul(sums[q][:, :], w2_parts[w][:, c, m * P:(m + 1) * P],
                                                h1_parts[x][:, c, :], start=(c == i == 0),
                                                stop=(c == m1 - 1 and i == len(PASSES) - 1))
                last.then_inc(summed_up[q], 1)

            def layer3(step):
                to = bank_of["layer3", 0]
                for c in range(m2):
                    q = bank_of["layer2", c]
                    pe.wait_ge(sums_out[q], use_number(step, "layer2", c, q) + 1)
                    last = nc.tensor.matmul(sums[to][0:1, :], w3[:, c:c + 1], h2[:, c, :],
                                            start=(c == 0), stop=(c == m2 - 1))
                last.then_inc(summed_up[to], 1)

            pe.wait_ge(ident_made, 2)

            def body(step, r, s, last_step=False):
                behind = not (isinstance(step, int) and step == 0)
                for j in range(K - 3 if behind else K):
                    onehot_sums(step, j)
                if not behind:
                    pe.wait_ge(pad_set, 1)
                for k in range(3):
                    transposes(step, 0, 2 * k)
                    transposes(step, 0, 2 * k + 1)
                    if behind:
                        onehot_sums(step, K - 3 + k, frees=(k == 2))
                if behind:
                    layer1(step, [0])
                dot_products(step, 0, frees=not behind)
                if last_step:
                    for i in range(NB):
                        transposes(step, 1, i)
                    dot_products(step, 1)
                if behind:
                    layer1(step, range(1, m1))
                for k in range(3):
                    if not last_step:
                        transposes(step, 1, 2 * k)
                        transposes(step, 1, 2 * k + 1)
                    if behind and k < m2:
                        layer2(step, k)
                if behind:
                    layer3(step)
                else:
                    pe.wait_ge(weights_cut, 2)
                if not last_step:
                    dot_products(step, 1)

            all_steps(pe, body)
            layer1(steps)
            layer2(steps, 0)
            layer2(steps, 1)
            layer3(steps)


def kernel(**inputs):
    import concourse.bacc as bacc
    from concourse.bass_utils import run_bass_kernel_spmd

    nc = bacc.Bacc("TRN2", target_bir_lowering=False, num_devices=1)
    given = dict(inputs, ids_summed=np.asarray(inputs["ids"]).T[list(SUMMED)])
    arrays, ins = {}, {}
    for name, value in given.items():
        a = np.ascontiguousarray(value)
        arrays[f"in_{name}"] = a
        ins[name] = nc.dram_tensor(f"in_{name}", a.shape, mybir.dt.from_np(a.dtype), kind="ExternalInput").ap()
    n = arrays["in_ids"].shape[0]
    out = nc.dram_tensor("out_y", (n, 1), F32, kind="ExternalOutput").ap()
    dlrm_kernel(nc, ins, out)
    return run_bass_kernel_spmd(nc, [arrays], core_ids=[0]).results[0]["out_y"]
```
